# Optimizing a Trainium2 kernel written in Bass

```python
import numpy as np
import jax
import jax.numpy as jnp

def _softmax(x, axis=-1):
    return jax.nn.softmax(x, axis=axis)

def _gelu(x):
    return jax.nn.gelu(x, approximate=True)

def _silu(x):
    return jax.nn.silu(x)

def _sigmoid(x):
    return jax.nn.sigmoid(x)

def _layernorm(x, axis=-1, eps=1e-05):
    m = jnp.mean(x, axis=axis, keepdims=True)
    v = jnp.var(x, axis=axis, keepdims=True)
    return (x - m) / jnp.sqrt(v + eps)

def _scatter_add(tgt, idx, src, axis=0):
    return tgt.at[idx].add(src)

def _segment_sum(src, seg, n):
    return jax.ops.segment_sum(src, seg, n)
kernel_name = 'mk_gnn_resnorm_d1_gnn_r32_854637'

def setup_inputs(seed: int=0):
    np.random.seed(seed)
    _w = jnp.asarray

    def _rec_inputs():
        import jax
        import jax.numpy as jnp
        _gk = jax.random.key(seed)
        x = -0.000202 + 1 * jax.random.normal(jax.random.fold_in(_gk, 1), (50000, 128), jnp.float32)
        src = jax.random.randint(jax.random.fold_in(_gk, 2), (25000,), 0, 50000, jnp.int32)
        dst = jax.random.randint(jax.random.fold_in(_gk, 3), (25000,), 0, 50000, jnp.int32)
        _o = jnp.argsort(dst, stable=True)
        src = src[_o]
        dst = dst[_o]
        edge_attr_128 = -5.16925e-05 + 1.00005 * jax.random.normal(jax.random.fold_in(_gk, 11), (25000, 128), jnp.float32)
        return (x, src, dst, edge_attr_128)
    x, src, dst, edge_attr_128 = _rec_inputs()

    def _L0_gnn_setup():
        import jax, jax.numpy as jnp
        import numpy as np
        N_NODES = 50000
        N_EDGES = 25000
        D = 128
        key = jax.random.key(seed)
        ks = jax.random.split(key, 6)
        node_feat = jax.random.normal(ks[0], (N_NODES, D), dtype=jnp.float32)
        edge_index = jax.random.randint(ks[1], (2, N_EDGES), 0, N_NODES, dtype=jnp.int64)
        edge_attr = jax.random.normal(ks[2], (N_EDGES, D), dtype=jnp.float32)
        W1 = jax.random.normal(ks[3], (D, 2 * D), dtype=jnp.float32) * (1.0 / np.sqrt(D))
        b1 = jnp.zeros((2 * D,), dtype=jnp.float32)
        W2 = jax.random.normal(ks[4], (2 * D, D), dtype=jnp.float32) * (1.0 / np.sqrt(2 * D))
        b2 = jnp.zeros((D,), dtype=jnp.float32)
        return {'node_feat': node_feat, 'edge_index': edge_index, 'edge_attr': edge_attr, 'W1': W1, 'b1': b1, 'W2': W2, 'b2': b2}
    _L0_gnn_all = _L0_gnn_setup()
    _L0_gnn_in = {k: v for k, v in _L0_gnn_all.items() if k in ('W1', 'b1', 'W2', 'b2')}
    del _L0_gnn_all
    return {'x': x, 'src': src, 'dst': dst, 'edge_attr_128': edge_attr_128, 'L0_gnn_W1': _L0_gnn_in['W1'], 'L0_gnn_b1': _L0_gnn_in['b1'], 'L0_gnn_W2': _L0_gnn_in['W2'], 'L0_gnn_b2': _L0_gnn_in['b2']}

def reference(x, src, dst, edge_attr_128, L0_gnn_W1, L0_gnn_b1, L0_gnn_W2, L0_gnn_b2):
    import jax
    import jax.numpy as jnp

    def _L0_gnn_ref(node_feat, edge_index, edge_attr, W1, b1, W2, b2):
        import jax, jax.numpy as jnp
        import numpy as np
        N_NODES = 50000
        N_EDGES = 25000
        D = 128
        src = edge_index[0]
        dst = edge_index[1]
        msg = jax.nn.relu(node_feat[src] + edge_attr)
        agg = jax.ops.segment_sum(msg, dst, num_segments=node_feat.shape[0])
        h = node_feat + agg
        h = jax.nn.relu(h @ W1 + b1) @ W2 + b2
        return jax.nn.relu(h)
    edge_index = jnp.stack([src, dst])
    x = _layernorm(x + _L0_gnn_ref(x, edge_index, edge_attr_128, L0_gnn_W1, L0_gnn_b1, L0_gnn_W2, L0_gnn_b2), axis=-1)
    return x

_drawn_inputs = setup_inputs


def setup_inputs(seed=0):
    import zlib

    import numpy as np

    out = dict(_drawn_inputs(seed))
    spreads = {'L0_gnn_b1': (0.0, 0.1), 'L0_gnn_b2': (0.0, 0.1)}
    factors = {}
    for name, (base, spread) in spreads.items():
        noise = np.random.default_rng([zlib.crc32(name.encode()), seed]).standard_normal(out[name].shape)
        drawn = base * np.exp(spread * noise) if base else spread * noise
        out[name] = jnp.asarray(drawn.astype(out[name].dtype))
    for name, factor in factors.items():
        out[name] = (out[name] * factor).astype(out[name].dtype)
    return out
```

```python
import concourse.bass as bass
from concourse import mybir
from contextlib import ExitStack

FP32 = mybir.dt.float32
BF16 = mybir.dt.bfloat16
INT32 = mybir.dt.int32
F32R = mybir.dt.float32r
UINT32 = mybir.dt.uint32
ALU = mybir.AluOpType
ACT = mybir.ActivationFunctionType
AX_X = mybir.AxisListType.X

LN_EPS = 1e-5


def wait_count(engine, semaphore, count):
    if not (isinstance(count, int) and count <= 0):
        engine.wait_ge(semaphore, count)


def general_path(nc, x, src, dst, edge_attr, out, h_dram, c, sb, pb, sem):
    nodes, D = x.shape
    edges = edge_attr.shape[0]
    HC = c["w2_sb"].shape[1]
    ET = 125
    NT = 125
    EDGE_TILES, NODE_TILES = edges // ET, nodes // NT
    assert EDGE_TILES * ET == edges and NODE_TILES * NT == nodes
    SKIP = float(1 << 20)

    src_col = sb("g_src_col", [ET, 1], INT32)
    dst_col = sb("g_dst_col", [ET, 1], INT32)
    dst_col_f = sb("g_dst_col_f", [ET, 1])
    ea = sb("g_ea", [ET, D])
    xsrc = sb("g_xsrc", [ET, D])
    pre_msg = sb("g_pre_msg", [ET, D])
    msg = sb("g_msg", [ET, D])
    pool_mark = sb("g_pool_mark", [1, 2])
    before = sb("g_before", [ET, ET])
    same = sb("g_same", [ET, ET])
    same_before = sb("g_same_before", [ET, ET])
    repeats = sb("g_repeats", [ET, 1])
    target_f = sb("g_target_f", [ET, 1])
    target = sb("g_target", [ET, 1], INT32)
    h_old = sb("g_h_old", [ET, D])
    h_new = sb("g_h_new", [ET, D])
    x_sb = sb("g_x", [NT, D])
    h_sb = sb("g_h", [NT, D])
    hT = sb("g_hT", [D, NT])
    h1T = sb("g_h1T", [128, HC, NT])
    z = sb("g_z", [NT, D])
    stats = sb("g_stats", [NT, 6])
    mean_var = sb("g_mean_var", [NT, 2])
    std = sb("g_std", [NT, 1])
    rstd = sb("g_rstd", [NT, 1])
    y = sb("g_y", [NT, D])

    copied = sem("g_copied")
    marks = sem("g_marks")
    before_ready = sem("g_before_ready")
    edges_loaded = sem("g_edges_loaded")
    xsrc_loaded = sem("g_xsrc_loaded")
    h_old_loaded = sem("g_h_old_loaded")
    dst_f_ready = sem("g_dst_f_ready")
    dst_row_ready = sem("g_dst_row_ready")
    same_ready = sem("g_same_ready")
    repeats_ready = sem("g_repeats_ready")
    masked = sem("g_masked")
    masked_target = sem("g_masked_target")
    target_ready = sem("g_target_ready")
    summed = sem("g_summed")
    msg_ready = sem("g_msg_ready")
    msg_summed = sem("g_msg_summed")
    h_new_ready = sem("g_h_new_ready")
    scattered = sem("g_scattered")
    tile_loaded = sem("g_tile_loaded")
    hT_ready = sem("g_hT_ready")
    hT_copied = sem("g_hT_copied")
    h1_summed = sem("g_h1_summed")
    h1_ready = sem("g_h1_ready")
    h2_summed = sem("g_h2_summed")
    z_ready = sem("g_z_ready")
    stats_ready = sem("g_stats_ready")
    var_ready = sem("g_var_ready")
    std_ready = sem("g_std_ready")
    rstd_ready = sem("g_rstd_ready")
    y_ready = sem("g_y_ready")
    stored = sem("g_stored")

    dst_row_ps, msg_ps, hT_ps, h1_ps, h2_ps = (c["prep_ps"][0], c["prep_ps"][1], c["banks"][0], c["banks"][1], c["banks"][2])

    with nc.Block() as block:
        @block.sync
        def _(sp):
            sp.dma_start(h_dram.rearrange("(a b) d -> a (b d)", b=NT), x.rearrange("(a b) d -> a (b d)", b=NT)).then_inc(copied, 16)

            def load_edges(first):
                sp.dma_start(src_col[:, :], src[bass.ds(first, ET)].rearrange("(p a) -> p a", a=1)).then_inc(edges_loaded, 16)
                sp.dma_start(dst_col[:, :], dst[bass.ds(first, ET)].rearrange("(p a) -> p a", a=1)).then_inc(edges_loaded, 16)
                sp.dma_start(ea[:, :], edge_attr[bass.ds(first, ET), :]).then_inc(edges_loaded, 16)

            load_edges(0)
            with sp.Fori(1, EDGE_TILES) as i:
                sp.wait_ge(scattered, i * 16)
                load_edges(i * ET)
            sp.wait_ge(scattered, EDGE_TILES * 16)

            def load_nodes(first):
                sp.dma_start(x_sb[:, :], x[bass.ds(first, NT), :]).then_inc(tile_loaded, 16)
                sp.dma_start(h_sb[:, :], h_dram[bass.ds(first, NT), :]).then_inc(tile_loaded, 16)

            load_nodes(0)
            with sp.Fori(1, NODE_TILES) as i:
                sp.wait_ge(y_ready, i)
                sp.dma_start(out[bass.ds((i - 1) * NT, NT), :], y[:, :]).then_inc(stored, 16)
                sp.wait_ge(stored, i * 16)
                load_nodes(i * NT)
            sp.wait_ge(y_ready, NODE_TILES)
            sp.dma_start(out[(NODE_TILES - 1) * NT:NODE_TILES * NT, :], y[:, :]).then_inc(stored, 16)
            sp.wait_ge(stored, NODE_TILES * 16)

        @block.gpsimd
        def _(pool):
            nc.gpsimd.memset(before[:, :], 0.0).then_inc(before_ready, 1)
            nc.gpsimd.memset(pool_mark[:, :], 0.0).then_inc(marks, 1)
            pool.wait_ge(marks, 1)
            pool.wait_ge(before_ready, 1)
            nc.gpsimd.affine_select(out=before[:, :], in_=before[:, :], compare_op=ALU.is_ge, fill=1.0,
                                    base=0, pattern=[[1, ET]], channel_multiplier=-1).then_inc(before_ready, 1)
            pool.wait_ge(copied, 16)

            def mark(done):
                pool.wait_ge(marks, done)
                nc.gpsimd.tensor_tensor(pool_mark[:, 1:2], pool_mark[:, 0:1], pool_mark[:, 0:1], ALU.add).then_inc(marks, 1)

            with pool.Fori(0, EDGE_TILES) as i:
                pool.wait_ge(edges_loaded, (i + 1) * 48)
                mark(2 * i + 1)
                nc.gpsimd.indirect_dma_start(out=xsrc[:, :], out_offset=None, in_=x,
                                             in_offset=bass.IndirectOffsetOnAxis(ap=src_col[:, 0:1], axis=0)).then_inc(xsrc_loaded, 16)
                nc.gpsimd.indirect_dma_start(out=h_old[:, :], out_offset=None, in_=h_dram,
                                             in_offset=bass.IndirectOffsetOnAxis(ap=dst_col[:, 0:1], axis=0)).then_inc(h_old_loaded, 16)
                pool.wait_ge(target_ready, i + 1)
                pool.wait_ge(h_new_ready, i + 1)
                mark(2 * i + 2)
                nc.gpsimd.indirect_dma_start(out=h_dram, out_offset=bass.IndirectOffsetOnAxis(ap=target[:, 0:1], axis=0),
                                             in_=h_new[:, :], in_offset=None,
                                             bounds_check=nodes - 1, oob_is_err=False).then_inc(scattered, 16)

        @block.vector
        def _(dve):
            dve.wait_ge(before_ready, 2)
            with dve.Fori(0, EDGE_TILES) as i:
                n = i + 1
                dve.wait_ge(edges_loaded, n * 48)
                nc.vector.tensor_copy(dst_col_f[:, :], dst_col[:, :]).then_inc(dst_f_ready, 1)
                dve.wait_ge(dst_f_ready, n)
                dve.wait_ge(dst_row_ready, n)
                nc.vector.tensor_scalar(same[:, :], dst_row_ps[0:ET, 0:ET], dst_col_f[:, 0:1], None, ALU.is_equal).then_inc(same_ready, 1)
                dve.wait_ge(same_ready, n)
                nc.vector.tensor_tensor(same_before[:, :], same[:, :], before[:, :], ALU.mult).then_inc(masked, 1)
                dve.wait_ge(masked, n)
                nc.vector.reduce_max(repeats[:, :], same_before[:, :], AX_X).then_inc(repeats_ready, 1)
                dve.wait_ge(repeats_ready, n)
                nc.vector.scalar_tensor_tensor(target_f[:, :], repeats[:, :], SKIP, dst_col_f[:, :], ALU.mult, ALU.add).then_inc(masked_target, 1)
                dve.wait_ge(masked_target, n)
                nc.vector.tensor_copy(target[:, :], target_f[:, :]).then_inc(target_ready, 1)
                dve.wait_ge(xsrc_loaded, n * 16)
                nc.vector.tensor_tensor(pre_msg[:, :], ea[:, :], xsrc[:, :], ALU.add).then_inc(summed, 1)
                dve.wait_ge(summed, n)
                nc.vector.tensor_scalar(msg[:, :], pre_msg[:, :], 0.0, None, ALU.max).then_inc(msg_ready, 1)
                dve.wait_ge(h_old_loaded, n * 16)
                dve.wait_ge(msg_summed, n)
                nc.vector.tensor_tensor(h_new[:, :], msg_ps[0:ET, 0:D], h_old[:, :], ALU.add).then_inc(h_new_ready, 1)
            with dve.Fori(0, NODE_TILES) as i:
                n = i + 1
                dve.wait_ge(tile_loaded, n * 32)
                dve.wait_ge(h2_summed, n)
                nc.vector.scalar_tensor_tensor(z[:, :], h2_ps[0:NT, 0, :], 0.0, x_sb[:, :], ALU.max, ALU.add).then_inc(z_ready, 1)
                dve.wait_ge(z_ready, n)
                nc.vector.bn_stats(stats[:, :], z[:, :]).then_inc(stats_ready, 1)
                dve.wait_ge(stats_ready, n)
                nc.vector.memset(rstd[:, :], 0.0)
                nc.vector.bn_aggr(mean_var[:, :], stats[:, :]).then_inc(var_ready, 1)
                dve.wait_ge(std_ready, n)
                nc.vector.reciprocal(rstd[:, :], std[:, :]).then_inc(rstd_ready, 1)
                dve.wait_ge(rstd_ready, n)
                nc.vector.tensor_scalar(y[:, :], z[:, :], mean_var[:, 0:1], rstd[:, 0:1], ALU.subtract, ALU.mult).then_inc(y_ready, 1)

        @block.scalar
        def _(act):
            with act.Fori(0, NODE_TILES) as i:
                n = i + 1
                act.wait_ge(hT_ready, n)
                nc.scalar.activation(hT[:, :], hT_ps[:, 0, 0:NT], ACT.Copy).then_inc(hT_copied, 1)
                act.wait_ge(h1_summed, n)
                for k in range(HC):
                    last = nc.scalar.activation(h1T[:, k, :], h1_ps[:, k, 0:NT], ACT.Relu, bias=c["b1_sb"][:, k:k + 1])
                last.then_inc(h1_ready, 1)
                act.wait_ge(var_ready, n)
                nc.scalar.activation(std[:, :], mean_var[:, 1:2], ACT.Sqrt, bias=c["eps_col"][0:NT, :]).then_inc(std_ready, 1)

        @block.tensor
        def _(pe):
            with pe.Fori(0, EDGE_TILES) as i:
                n = i + 1
                pe.wait_ge(dst_f_ready, n)
                nc.tensor.matmul(dst_row_ps[0:ET, 0:ET], dst_col_f[:, 0:1].to_broadcast([ET, ET]), c["ident"][0:ET, 0:ET],
                                 start=True, stop=True).then_inc(dst_row_ready, 1)
                pe.wait_ge(same_ready, n)
                pe.wait_ge(msg_ready, n)
                nc.tensor.matmul(msg_ps[0:ET, 0:D], same[:, :], msg[:, :], start=True, stop=True).then_inc(msg_summed, 1)
            with pe.Fori(0, NODE_TILES) as i:
                n = i + 1
                pe.wait_ge(tile_loaded, n * 32)
                nc.tensor.transpose(hT_ps[:, 0, 0:NT], h_sb[:, :], c["ident"][0:NT, 0:NT]).then_inc(hT_ready, 1)
                pe.wait_ge(hT_copied, n)
                for k in range(HC):
                    last = nc.tensor.matmul(h1_ps[:, k, 0:NT], c["w1_sb"][:, k * 128:(k + 1) * 128], hT[:, :], start=True, stop=True)
                last.then_inc(h1_summed, 1)
                nc.tensor.matmul(h2_ps[0:NT, 0, :], c["ones3"][:, 0:NT], c["b2_parts"][:, 0:D], start=True, stop=False)
                pe.wait_ge(h1_ready, n)
                for k in range(HC):
                    last = nc.tensor.matmul(h2_ps[0:NT, 0, :], h1T[:, k, :], c["w2_sb"][:, k, :], start=False, stop=(k == HC - 1))
                last.then_inc(h2_summed, 1)


def gnn_resnorm_kernel(nc, x, src, dst, edge_attr, w1, b1, w2, b2, out, window_table, h_dram):
    nodes, D = x.shape
    edges = edge_attr.shape[0]
    hidden = w1.shape[1]
    HC = hidden // 128

    T = 4
    G = 128 * T
    GROUPS = -(-nodes // G)
    LAST_BASE = nodes - G

    K = 3
    P0 = [0, 44, 86, 128]
    WP = max(P0[k + 1] - P0[k] for k in range(K))
    EW = 128
    LAST_WINDOW = edges - EW

    ROWS = 100
    ROW = edges // ROWS
    assert ROWS * ROW == edges and ROWS <= 128 and GROUPS <= 128

    U = 4
    X_AHEAD, EA_AHEAD = 3, 6
    LOOPS = (GROUPS - EA_AHEAD) // U
    STEPS_LEFT = range(LOOPS * U, GROUPS)

    x_dma = lambda base: x[bass.ds(base, G), :].rearrange("(p t) d -> p t d", t=T)
    out_dma = lambda base: out[bass.ds(base, G), :].rearrange("(p t) d -> p t d", t=T)

    ctx = ExitStack()
    with ctx:
        def sb(name, shape, dt=FP32):
            return ctx.enter_context(nc.sbuf_tensor(name, shape, dt))

        def pb(name, shape, dt=FP32):
            return ctx.enter_context(nc.psum_tensor(name, shape, dt))

        def sem(name):
            return ctx.enter_context(nc.semaphore(name))

        ident = sb("ident", [128, 128])
        ones_col = sb("ones_col", [128, 1])
        w1_sb = sb("w1_sb", [128, hidden])
        w2_sb = sb("w2_sb", [128, HC, D])
        b1_sb = sb("b1_sb", [128, HC])
        b2_row = sb("b2_row", [1, D])
        b2_rest = sb("b2_rest", [1, 2, D])
        b2_cut = sb("b2_cut", [1, 3, T, D], BF16)
        b2_parts = sb("b2_parts", [3, T * D], BF16)
        ones3 = sb("ones3", [3, 128], BF16)
        node_in_range = sb("node_in_range", [128, 1, T * WP])
        eps_col = sb("eps_col", [128, 1])

        dst_rows = sb("dst_rows", [ROWS, ROW + 1], INT32)
        dst_rows_f = sb("dst_rows_f", [ROWS, ROW + 1])
        unsorted = sb("unsorted", [ROWS, ROW])
        range_node = sb("range_node", [GROUPS, K + 1])
        row_count = sb("row_count", [GROUPS, K + 1])
        row_index = sb("row_index", [GROUPS, K + 1], INT32)
        before = sb("before", [GROUPS, ROW])
        found_row = sb("found_row", [GROUPS, K + 1, ROW], INT32)
        in_row = sb("in_row", [GROUPS, K + 1])
        edge_start = sb("edge_start", [GROUPS, K + 1])
        window_start = sb("window_start", [GROUPS, K])
        window_start_i = sb("window_start_i", [GROUPS, K], INT32)
        src_win = sb("src_win", [GROUPS, K, EW], INT32)
        dst_win = sb("dst_win", [GROUPS, K, EW], INT32)
        src_win_f = sb("src_win_f", [GROUPS, K, EW])
        dst_win_f = sb("dst_win_f", [GROUPS, K, EW])
        src_of = sb("src_of", [128, GROUPS, K], INT32)
        dst_of = sb("dst_of", [128, GROUPS, K])
        too_many = sb("too_many", [GROUPS, K])
        violations = sb("violations", [128, 2])
        general_f = sb("general_f", [1, 1])
        general = sb("general", [1, 1], INT32)
        starts_row = sb("starts_row", [1, GROUPS * K], INT32)

        x_sb = sb("x_sb", [128, U, T, D])
        ea_sb = sb("ea_sb", [128, U, K, D])
        src_idx = sb("src_idx", [128, U, K], INT32)
        xsrc_sb = sb("xsrc_sb", [128, U, K, D])
        pre_msg = sb("pre_msg", [128, U, K, D])
        msg_hi = sb("msg_hi", [128, U, K, D], F32R)
        msg_lo = sb("msg_lo", [128, U, K, D], F32R)
        sel = sb("sel", [128, U, K, T * WP], F32R)
        hT = sb("hT", [128, T, 128])
        h1T = sb("h1T", [128, HC, T, 128])
        z = sb("z", [128, U, T, D])
        y = sb("y", [128, U, T, D])
        stats = sb("stats", [128, U, T, 6])
        mean_var = sb("mean_var", [128, U, T, 2])
        std = sb("std", [128, U, T])
        rstd = sb("rstd", [128, U, T])
        shift = sb("shift", [128, U, T])

        hT_ps = pb("hT_ps", [128, T, 128])
        h1T_ps = [pb(f"h1T_ps{c}", [128, T, 128]) for c in range(HC)]
        h2_ps = [pb(f"h2_ps{i}", [128, T, D]) for i in range(2)]
        prep_ps = [pb(f"prep_ps{i}", [128, 512]) for i in range(2)]

        weights_loaded = sem("weights_loaded")
        dst_loaded = sem("dst_loaded")
        pool_consts = sem("pool_consts")
        ident_ready = sem("ident_ready")
        vec = sem("vec")
        dst_f_ready = sem("dst_f_ready")
        last_of_rows = sem("last_of_rows")
        row_index_ready = sem("row_index_ready")
        rows_found = sem("rows_found")
        starts_ready = sem("starts_ready")
        starts_loaded = sem("starts_loaded")
        windows_loaded = sem("windows_loaded")
        window_f_ready = sem("window_f_ready")
        window_T_ready = sem("window_T_ready")
        window_T_copied = sem("window_T_copied")
        general_ready = sem("general_ready")
        violations_ready = sem("violations_ready")
        violations_summed = sem("violations_summed")
        b2_cut_ready = sem("b2_cut_ready")
        b2_parts_loaded = sem("b2_parts_loaded")

        x_loaded = [sem(f"x_loaded{u}") for u in range(U)]
        ea_loaded = [sem(f"ea_loaded{u}") for u in range(U)]
        xsrc_loaded = [sem(f"xsrc_loaded{u}") for u in range(U)]
        out_stored = [sem(f"out_stored{u}") for u in range(U)]
        idx_copied = sem("idx_copied")
        summed = sem("summed")
        msg_hi_ready = sem("msg_hi_ready")
        msg_lo_ready = sem("msg_lo_ready")
        sel_ready = sem("sel_ready")
        hT_summed = sem("hT_summed")
        hT_copied = sem("hT_copied")
        h1_summed = sem("h1_summed")
        h1_ready = sem("h1_ready")
        h2_summed = sem("h2_summed")
        z_ready = sem("z_ready")
        stats_ready = sem("stats_ready")
        var_ready = sem("var_ready")
        std_ready = sem("std_ready")
        rstd_ready = sem("rstd_ready")
        shift_ready = sem("shift_ready")
        y_ready = sem("y_ready")

        def group_base(g):
            return LAST_BASE if isinstance(g, int) and g == GROUPS - 1 else g * G

        def steps(engine, step):
            for u in range(U):
                step(u, u, 0)
            with engine.Fori(1, LOOPS) as i:
                for u in range(U):
                    step(i * U + u, u, i)
            for g in STEPS_LEFT:
                step(g, g % U, g // U)

        with nc.Block() as block:
            @block.sync
            def _(sp):
                sp.dma_start(dst_rows[0:ROWS - 1, :],
                             bass.AP(dst.tensor, 0, [[ROW, ROWS - 1], [1, ROW + 1]])).then_inc(dst_loaded, 16)
                sp.dma_start(dst_rows[ROWS - 1:ROWS, 0:ROW],
                             dst[edges - ROW:edges].rearrange("(a e) -> a e", a=1)).then_inc(dst_loaded, 16)
                sp.dma_start(dst_rows[ROWS - 1:ROWS, ROW:ROW + 1],
                             dst[edges - 1:edges].rearrange("(a e) -> a e", a=1)).then_inc(dst_loaded, 16)
                sp.dma_start(w1_sb[:, :], w1).then_inc(weights_loaded, 16)
                sp.dma_start(w2_sb[:, :, :], w2.rearrange("(c p) n -> p c n", p=128)).then_inc(weights_loaded, 16)
                for c in range(HC):
                    sp.dma_start(b1_sb[:, c:c + 1], b1[c * 128:(c + 1) * 128].rearrange("(p a) -> p a", a=1)).then_inc(weights_loaded, 16)
                sp.dma_start(b2_row[:, :], b2.rearrange("(a n) -> a n", a=1)).then_inc(weights_loaded, 16)
                sp.wait_ge(b2_cut_ready, 1)
                for i in range(3):
                    sp.dma_start(b2_parts[i:i + 1, :], b2_cut[0:1, i, :, :].rearrange("a t n -> a (t n)")).then_inc(b2_parts_loaded, 16)

                sp.wait_ge(starts_ready, 1)
                sp.dma_start(window_table, window_start_i[:, :]).then_inc(starts_loaded, 16)
                sp.wait_ge(starts_loaded, 16)
                sp.dma_start(starts_row[:, :], window_table.rearrange("(a g) k -> a (g k)", a=1)).then_inc(starts_loaded, 16)
                sp.wait_ge(starts_loaded, 32)
                sp.wait_ge(weights_loaded, 16 * (3 + HC))
                sp.wait_ge(b2_parts_loaded, 16 * 3)

            @block.gpsimd
            def _(pool):
                nc.gpsimd.memset(ident[:, :], 0.0).then_inc(pool_consts, 1)
                pool.wait_ge(pool_consts, 1)
                nc.gpsimd.affine_select(out=ident[:, :], in_=ident[:, :], compare_op=ALU.not_equal, fill=1.0,
                                        base=0, pattern=[[-1, 128]], channel_multiplier=1).then_inc(ident_ready, 1)
                for k in range(K + 1):
                    nc.gpsimd.iota(range_node[:, k:k + 1], pattern=[[0, 1]], base=0, channel_multiplier=G,
                                   allow_small_or_imprecise_dtypes=True).then_inc(pool_consts, 1)
                nc.gpsimd.iota(node_in_range[:, 0, :].rearrange("p (t q) -> p t q", t=T), pattern=[[1, T], [T, WP]], base=0, channel_multiplier=0,
                               allow_small_or_imprecise_dtypes=True).then_inc(pool_consts, 1)
                pool.wait_ge(row_index_ready, 1)
                for k in range(K + 1):
                    nc.gpsimd.indirect_dma_start(
                        out=found_row[:, k, :], out_offset=None, in_=dst.rearrange("(r e) -> r e", e=ROW),
                        in_offset=bass.IndirectOffsetOnAxis(ap=row_index[:, k:k + 1], axis=0)).then_inc(rows_found, 16)
                pool.wait_ge(starts_ready, 1)
                for k in range(K):
                    for vec_dram, win in ((src, src_win), (dst, dst_win)):
                        nc.gpsimd.indirect_dma_start(
                            out=win[:, k, :], out_offset=None, in_=vec_dram.rearrange("(e a) -> e a", a=1),
                            in_offset=bass.IndirectOffsetOnAxis(ap=window_start_i[:, k:k + 1], axis=0)).then_inc(windows_loaded, 16)

            @block.vector
            def _(dve):
                chain = [0]

                def link(ins):
                    chain[0] += 1
                    ins.then_inc(vec, 1)
                    dve.wait_ge(vec, chain[0])

                nc.vector.memset(ones3[:, :], 1.0)
                nc.vector.memset(eps_col[:, :], LN_EPS)
                link(nc.vector.memset(ones_col[:, :], 1.0))
                dve.wait_ge(dst_loaded, 48)
                nc.vector.tensor_copy(dst_rows_f[:, :], dst_rows[:, :]).then_inc(dst_f_ready, 1)
                dve.wait_ge(pool_consts, K + 3)
                for k in range(K + 1):
                    last = nc.vector.tensor_scalar(range_node[:, k:k + 1], range_node[:, k:k + 1], float(LAST_BASE), float(T * P0[k]),
                                                   ALU.min, ALU.add)
                link(last)
                dve.wait_ge(last_of_rows, 1)
                for k in range(K + 1):
                    link(nc.vector.tensor_scalar(before[:, 0:ROWS], prep_ps[0][0:GROUPS, 0:ROWS], range_node[:, k:k + 1], None,
                                                 ALU.is_lt, ALU.add, accum_out=row_count[:, k:k + 1]))
                link(nc.vector.tensor_scalar(row_count[:, :], row_count[:, :], float(ROWS - 1), None, ALU.min))
                nc.vector.tensor_copy(row_index[:, :], row_count[:, :]).then_inc(row_index_ready, 1)
                dve.wait_ge(rows_found, 16 * (K + 1))
                for k in range(K + 1):
                    link(nc.vector.tensor_copy(before[:, :], found_row[:, k, :]))
                    link(nc.vector.tensor_scalar(before[:, :], before[:, :], range_node[:, k:k + 1], None,
                                                 ALU.is_lt, ALU.add, accum_out=in_row[:, k:k + 1]))
                link(nc.vector.scalar_tensor_tensor(edge_start[:, :], row_count[:, :], float(ROW), in_row[:, :], ALU.mult, ALU.add))
                link(nc.vector.tensor_scalar(window_start[:, :], edge_start[:, 0:K], float(LAST_WINDOW), None, ALU.min))
                nc.vector.tensor_copy(window_start_i[:, :], window_start[:, :]).then_inc(starts_ready, 1)
                link(nc.vector.memset(violations[:, :], 0.0))
                nc.vector.tensor_tensor(unsorted[:, :], dst_rows_f[:, 0:ROW], dst_rows_f[:, 1:ROW + 1], ALU.is_gt)
                link(nc.vector.tensor_tensor(too_many[:, :], edge_start[:, 1:K + 1], window_start[:, :], ALU.subtract))
                link(nc.vector.tensor_scalar(too_many[:, :], too_many[:, :], float(EW), None, ALU.is_gt))
                nc.vector.reduce_max(violations[0:ROWS, 0:1], unsorted[:, :], AX_X)
                nc.vector.reduce_max(violations[0:GROUPS, 1:2], too_many[:, :], AX_X).then_inc(violations_ready, 1)
                dve.wait_ge(violations_summed, 1)
                link(nc.vector.reduce_max(general_f[:, :], prep_ps[1][0:1, 0:2], AX_X))
                nc.vector.tensor_copy(general[:, :], general_f[:, :]).then_inc(general_ready, 1)
                dve.wait_ge(weights_loaded, 16 * (3 + HC))
                link(nc.vector.tensor_copy(b2_cut[:, 0, 0, :], b2_row[:, :]))
                link(nc.vector.tensor_tensor(b2_rest[:, 0, :], b2_row[:, :], b2_cut[:, 0, 0, :], ALU.subtract))
                link(nc.vector.tensor_copy(b2_cut[:, 1, 0, :], b2_rest[:, 0, :]))
                link(nc.vector.tensor_tensor(b2_rest[:, 1, :], b2_rest[:, 0, :], b2_cut[:, 1, 0, :], ALU.subtract))
                link(nc.vector.tensor_copy(b2_cut[:, 2, 0, :], b2_rest[:, 1, :]))
                for t in range(1, T):
                    last = nc.vector.tensor_copy(b2_cut[:, :, t, :], b2_cut[:, :, 0, :])
                last.then_inc(b2_cut_ready, 1)
                dve.wait_ge(windows_loaded, 16 * 2 * K)
                for k in range(K):
                    nc.vector.tensor_copy(src_win_f[:, k, :], src_win[:, k, :])
                    link(nc.vector.tensor_copy(dst_win_f[:, k, :], dst_win[:, k, :]))
                    nc.vector.tensor_scalar(dst_win_f[:, k, :], dst_win_f[:, k, :], range_node[:, k:k + 1], None,
                                            ALU.subtract).then_inc(window_f_ready, 1)
                for k in range(K):
                    dve.wait_ge(window_T_ready, k + 1)
                    ps = prep_ps[k % 2]
                    nc.vector.tensor_copy(src_of[:, :, k], ps[:, 0:GROUPS])
                    last = nc.vector.tensor_copy(dst_of[:, :, k], ps[:, GROUPS:2 * GROUPS])
                    last.then_inc(window_T_copied, 1)

            @block.tensor
            def _(pe):
                pe.wait_ge(ident_ready, 1)
                pe.wait_ge(dst_f_ready, 1)
                nc.tensor.matmul(prep_ps[0][0:GROUPS, 0:ROWS], dst_rows_f[:, ROW - 1:ROW].to_broadcast([ROWS, GROUPS]),
                                 ident[0:ROWS, 0:ROWS], start=True, stop=True).then_inc(last_of_rows, 1)
                pe.wait_ge(violations_ready, 1)
                nc.tensor.matmul(prep_ps[1][0:1, 0:2], ones_col[:, :], violations[:, :], start=True, stop=True).then_inc(violations_summed, 1)
                pe.wait_ge(general_ready, 1)
                for k in range(K):
                    pe.wait_ge(window_f_ready, k + 1)
                    wait_count(pe, window_T_copied, k - 1)
                    nc.tensor.transpose(prep_ps[k % 2][:, 0:GROUPS], src_win_f[:, k, :], ident[0:GROUPS, 0:GROUPS])
                    nc.tensor.transpose(prep_ps[k % 2][:, GROUPS:2 * GROUPS], dst_win_f[:, k, :], ident[0:GROUPS, 0:GROUPS]).then_inc(window_T_ready, 1)


        windows_fail = nc.values_load(general[0:1, 0:1], min_val=0, max_val=128)
        with nc.If(windows_fail == 0):
            with nc.Block() as block:
                @block.sync
                def _(sp):
                    def load_x(g, slot):
                        if not (isinstance(g, int) and g < U):
                            sp.wait_ge(z_ready, g - (U - 1))
                        sp.dma_start(x_sb[:, slot, :, :], x_dma(group_base(g))).then_inc(x_loaded[slot], 16)

                    def load_ea(g, slot):
                        if not (isinstance(g, int) and g < U):
                            sp.wait_ge(summed, g - (U - 1))
                        for k in range(K):
                            start = sp.value_load(starts_row[0:1, bass.ds(g * K + k, 1)], min_val=0, max_val=LAST_WINDOW)
                            sp.dma_start(ea_sb[:, slot, k, :], edge_attr[bass.ds(start, EW), :]).then_inc(ea_loaded[slot], 16)

                    for g in range(X_AHEAD):
                        load_x(g, g)
                    for g in range(EA_AHEAD):
                        load_ea(g, g % U)

                    def step(g, slot, n):
                        if not isinstance(g, int) or g + EA_AHEAD < GROUPS:
                            load_ea(g + EA_AHEAD, (slot + EA_AHEAD) % U)
                        if not isinstance(g, int) or g + X_AHEAD < GROUPS:
                            load_x(g + X_AHEAD, (slot + X_AHEAD) % U)
                        if not isinstance(g, int) or g >= 3:
                            store(g - 3, (slot + 1) % U)

                    def store(g, slot):
                        sp.wait_ge(y_ready, g + 1)
                        if isinstance(g, int) and g == GROUPS - 1:
                            sp.wait_ge(out_stored[(slot - 1) % U], 16 * ((g - 1) // U + 1))
                        sp.dma_start(out_dma(group_base(g)), y[:, slot, :, :]).then_inc(out_stored[slot], 16)

                    steps(sp, step)
                    for g in range(GROUPS - 3, GROUPS):
                        store(g, g % U)
                    for slot in range(U):
                        sp.wait_ge(out_stored[slot], 16 * len(range(slot, GROUPS, U)))

                @block.gpsimd
                def _(pool):
                    def copy_indices(g, slot):
                        nc.gpsimd.tensor_copy(src_idx[:, slot, :], src_of[:, bass.ds(g, 1), :].rearrange("p a k -> p (a k)")).then_inc(idx_copied, 1)

                    def gather(g, slot, n):
                        if not (isinstance(g, int) and g < U):
                            pool.wait_ge(summed, g - (U - 1))
                        pool.wait_ge(idx_copied, g + 1)
                        if not isinstance(g, int) or g + 1 < GROUPS:
                            if not (isinstance(g, int) and g + 1 < U):
                                pool.wait_ge(xsrc_loaded[(slot + 1) % U], (n if slot < U - 1 else n + 1) * (16 * K))
                            copy_indices(g + 1, (slot + 1) % U)
                        for k in range(K):
                            nc.gpsimd.indirect_dma_start(
                                out=xsrc_sb[:, slot, k, :], out_offset=None, in_=x,
                                in_offset=bass.IndirectOffsetOnAxis(ap=src_idx[:, slot, k:k + 1], axis=0)).then_inc(xsrc_loaded[slot], 16)
                    copy_indices(0, 0)
                    steps(pool, gather)

                @block.vector
                def _(dve):
                    def edge_sums(g, slot, n):
                        if not (isinstance(g, int) and g < U):
                            dve.wait_ge(hT_summed, g - (U - 1))
                        nc.vector.tensor_tensor(sel[:, slot, :, :], node_in_range[:, :, :].to_broadcast([128, K, T * WP]),
                                                dst_of[:, bass.ds(g, 1), :].rearrange("p a k -> p k a").to_broadcast([128, K, T * WP]),
                                                ALU.is_equal).then_inc(sel_ready, 1)
                        dve.wait_ge(ea_loaded[slot], (n + 1) * (16 * K))
                        dve.wait_ge(xsrc_loaded[slot], (n + 1) * (16 * K))
                        nc.vector.tensor_tensor(pre_msg[:, slot, :, :], ea_sb[:, slot, :, :], xsrc_sb[:, slot, :, :],
                                                ALU.add).then_inc(summed, 1)

                    def low_part(g, slot):
                        dve.wait_ge(msg_hi_ready, g + 1)
                        nc.vector.scalar_tensor_tensor(msg_lo[:, slot, :, :], pre_msg[:, slot, :, :], 0.0, msg_hi[:, slot, :, :].bitcast(FP32),
                                                       ALU.max, ALU.subtract).then_inc(msg_lo_ready, 1)

                    def add_and_stats(g, slot, n):
                        if not (isinstance(g, int) and g < U):
                            dve.wait_ge(y_ready, g - (U - 1))
                        dve.wait_ge(h2_summed, g + 1)
                        nc.vector.scalar_tensor_tensor(z[:, slot, :, :], h2_ps[slot % 2][:, :, :], 0.0, x_sb[:, slot, :, :],
                                                       ALU.max, ALU.add).then_inc(z_ready, 1)
                        dve.wait_ge(z_ready, g + 1)
                        for t in range(T):
                            last = nc.vector.bn_stats(stats[:, slot, t, :], z[:, slot, t, :])
                        last.then_inc(stats_ready, 1)
                        dve.wait_ge(stats_ready, g + 1)

                    def reciprocal(g, slot):
                        dve.wait_ge(std_ready, g + 1)
                        nc.vector.reciprocal(rstd[:, slot, :], std[:, slot, :]).then_inc(rstd_ready, 1)

                    def variance(g, slot):
                        for t in range(T):
                            last = nc.vector.bn_aggr(mean_var[:, slot, t, :], stats[:, slot, t, :])
                        last.then_inc(var_ready, 1)

                    def shifts(g, slot):
                        dve.wait_ge(rstd_ready, g + 1)
                        nc.vector.scalar_tensor_tensor(shift[:, slot, :], mean_var[:, slot, :, 0], -1.0, rstd[:, slot, :],
                                                       ALU.mult, ALU.mult).then_inc(shift_ready, 1)

                    for g in range(3):
                        edge_sums(g, g, 0)
                    for g in range(2):
                        low_part(g, g)

                    def step(g, slot, n):
                        if not isinstance(g, int) or g + 3 < GROUPS:
                            edge_sums(g + 3, (slot + 3) % U, n if slot < 1 else n + 1)
                        if not isinstance(g, int) or g + 2 < GROUPS:
                            low_part(g + 2, (slot + 2) % U)
                        add_and_stats(g, slot, n)
                        if not isinstance(g, int) or g >= 1:
                            reciprocal(g - 1, (slot - 1) % U)
                        variance(g, slot)
                        if not isinstance(g, int) or g >= 1:
                            shifts(g - 1, (slot - 1) % U)
                    steps(dve, step)
                    reciprocal(GROUPS - 1, (GROUPS - 1) % U)
                    shifts(GROUPS - 1, (GROUPS - 1) % U)

                @block.scalar
                def _(act):
                    def high_part(g, slot):
                        act.wait_ge(summed, g + 1)
                        if not (isinstance(g, int) and g < U):
                            act.wait_ge(hT_summed, g - (U - 1))
                        nc.scalar.activation(msg_hi[:, slot, :, :], pre_msg[:, slot, :, :], ACT.Relu).then_inc(msg_hi_ready, 1)

                    def copy_hT(g):
                        act.wait_ge(hT_summed, g + 1)
                        nc.scalar.activation(hT[:, :, :], hT_ps[:, :, :], ACT.Copy).then_inc(hT_copied, 1)

                    def hidden(g):
                        for c in range(HC):
                            act.wait_ge(h1_summed, g * HC + c + 1)
                            nc.scalar.activation(h1T[:, c, :, :], h1T_ps[c][:, :, :], ACT.Relu, bias=b1_sb[:, c:c + 1]).then_inc(h1_ready, 1)

                    def deviation(g, slot):
                        act.wait_ge(var_ready, g + 1)
                        nc.scalar.activation(std[:, slot, :], mean_var[:, slot, :, 1], ACT.Sqrt, bias=eps_col[:, :]).then_inc(std_ready, 1)

                    def normalize(g, slot, n):
                        act.wait_ge(shift_ready, g + 1)
                        if not (isinstance(g, int) and g < U):
                            act.wait_ge(out_stored[slot], n * 16)
                        for t in range(T):
                            last = nc.scalar.activation(y[:, slot, t, :], z[:, slot, t, :], ACT.Identity,
                                                        bias=shift[:, slot, t:t + 1], scale=rstd[:, slot, t:t + 1])
                        last.then_inc(y_ready, 1)

                    for g in range(2):
                        high_part(g, g)
                    copy_hT(0)
                    high_part(2, 2)

                    def step(g, slot, n):
                        hidden(g)
                        if not isinstance(g, int) or g + 1 < GROUPS:
                            copy_hT(g + 1)
                        if not isinstance(g, int) or g >= 1:
                            deviation(g - 1, (slot - 1) % U)
                        if not isinstance(g, int) or g + 3 < GROUPS:
                            high_part(g + 3, (slot + 3) % U)
                        if not isinstance(g, int) or g >= 2:
                            normalize(g - 2, (slot - 2) % U, n if slot >= 2 else n - 1)
                    steps(act, step)
                    deviation(GROUPS - 1, (GROUPS - 1) % U)
                    for g in (GROUPS - 2, GROUPS - 1):
                        normalize(g, g % U, g // U)

                @block.tensor
                def _(pe):
                    def sum_hT(g, slot, n):
                        pe.wait_ge(x_loaded[slot], (n + 1) * 16)
                        for t in range(T):
                            nc.tensor.matmul(hT_ps[:, t, :], x_sb[:, slot, t, :], ident[:, :], is_transpose=True,
                                             start=(t == 0), stop=False, skip_group_check=True)
                        pe.wait_ge(sel_ready, g + 1)
                        pe.wait_ge(msg_hi_ready, g + 1)
                        pe.wait_ge(msg_lo_ready, g + 1)
                        for k in range(K):
                            p0, p1 = P0[k], P0[k + 1]
                            cols = sel[:, slot, k, :].rearrange("p (t q) -> p t q", t=T)[:, :, 0:p1 - p0]
                            for part in (msg_hi, msg_lo):
                                last = nc.tensor.matmul(hT_ps[:, :, p0:p1], part[:, slot, k, :], cols,
                                                        start=False, stop=(k == K - 1), skip_group_check=True)
                        last.then_inc(hT_summed, 1)

                    sum_hT(0, 0, 0)

                    def step(g, slot, n):
                        pe.wait_ge(hT_copied, g + 1)
                        for c in range(HC):
                            nc.tensor.matmul(h1T_ps[c][:, :, :], w1_sb[:, c * 128:(c + 1) * 128], hT[:, :, :],
                                             start=True, stop=True).then_inc(h1_summed, 1)
                        if not isinstance(g, int) or g + 1 < GROUPS:
                            sum_hT(g + 1, (slot + 1) % U, n if slot + 1 < U else n + 1)
                        if not isinstance(g, int) or g >= 2:
                            pe.wait_ge(z_ready, g - 1)
                        h2 = h2_ps[slot % 2]
                        nc.tensor.matmul(h2[:, :, :], ones3[:, :], b2_parts[:, :], start=True, stop=False, skip_group_check=True)
                        for c in range(HC):
                            pe.wait_ge(h1_ready, g * HC + c + 1)
                            for t in range(T):
                                last = nc.tensor.matmul(h2[:, t, :], h1T[:, c, t, :], w2_sb[:, c, :],
                                                        start=False, stop=(c == HC - 1), skip_group_check=True)
                        last.then_inc(h2_summed, 1)
                    steps(pe, step)



        with nc.Else():
            consts = dict(ident=ident, w1_sb=w1_sb, w2_sb=w2_sb, b1_sb=b1_sb, ones3=ones3, b2_parts=b2_parts, eps_col=eps_col,
                                     prep_ps=prep_ps, banks=[hT_ps, h1T_ps[0], h1T_ps[1]])
            general_path(nc, x, src, dst, edge_attr, out, h_dram, consts, sb, pb, sem)

_INS = ["x", "src", "dst", "edge_attr_128", "L0_gnn_W1", "L0_gnn_b1", "L0_gnn_W2", "L0_gnn_b2"]


def kernel(**inputs):
    import numpy as _np
    import concourse.bacc as _bacc
    from concourse import mybir as _mybir
    from concourse.bass_utils import run_bass_kernel_spmd as _run

    nc = _bacc.Bacc("TRN2", target_bir_lowering=False, num_devices=1)
    arrays, args = {}, []
    for name in _INS:
        a = _np.ascontiguousarray(inputs[name])
        arrays[f"in_{name}_dram"] = a
        args.append(nc.dram_tensor(f"in_{name}_dram", a.shape, _mybir.dt.from_np(a.dtype), kind="ExternalInput").ap())
    shape = inputs["x"].shape
    out = nc.dram_tensor("out_dram", shape, _mybir.dt.float32, kind="ExternalOutput").ap()
    window_table = nc.dram_tensor("window_table", (98, 3), _mybir.dt.int32, kind="Internal").ap()
    h_dram = nc.dram_tensor("h_dram", shape, _mybir.dt.float32, kind="Internal").ap()
    gnn_resnorm_kernel(nc, *args, out, window_table, h_dram)
    r = _run(nc, [arrays], core_ids=[0])
    return r.results[0]["out_dram"]
```

```python
import concourse.bass as bass
from concourse import mybir
from contextlib import ExitStack

FP32 = mybir.dt.float32
FP32R = mybir.dt.float32r
INT32 = mybir.dt.int32
ALU = mybir.AluOpType
ACT = mybir.ActivationFunctionType
AX_X = mybir.AxisListType.X

LN_EPS = 1e-5

T = 4
G = 128 * T
P0 = [0, 44, 86, 128]
K = len(P0) - 1
WP = max(P0[k + 1] - P0[k] for k in range(K))
EW = 128
ROWS = 100


def known(g):
    return isinstance(g, int)


U = 4
X_AHEAD, EA_AHEAD = 3, 5
EA_FIRST = 1


def rows(dram, g, c):
    base = c["LAST_BASE"] if known(g) and g == c["GROUPS"] - 1 else g * G
    return dram[bass.ds(base, G), :].rearrange("(p t) d -> p t d", t=T)


def window_starts(nc, g, c):
    _, starts = nc.values_load_multi_w_load_instructions(
        c["starts_row"][0:1, bass.ds(g, 1), 0:K].rearrange("a g k -> a (g k)"), engines=(mybir.EngineType.SP,),
        min_val=0, max_val=c["LAST_WINDOW"])
    return starts


def start_x(sp, x, g, slot, c):
    sp.dma_start(c["x_sb"][:, slot, :, :], rows(x, g, c)).then_inc(c["x_loaded"][slot], 16)


def start_edge_attr(sp, edge_attr, starts, slot, c):
    for k in range(K):
        sp.dma_start(c["pre_msg"][:, slot, k, :], edge_attr[bass.ds(starts[k], EW), :]).then_inc(c["ea_loaded"][slot], 16)


def prepare(nc, x, edge_attr, dst, pairs, w1, b1, w2, b2, c, sb, sem):
    edges, = dst.shape
    ROW = edges // ROWS
    GROUPS, LAST_BASE, LAST_WINDOW, HC = c["GROUPS"], c["LAST_BASE"], c["LAST_WINDOW"], c["HC"]
    assert ROWS * ROW == edges and max(ROWS, GROUPS) <= 128
    ident, eps_col, b2_sb, node_in_range = c["ident"], c["eps_col"], c["b2_sb"], c["node_in_range"]
    prep_ps = c["prep_ps"]
    window_ps = [c["h2_ps"][0], c["h2_ps"][1], c["h1T_ps"][0]]

    ones_col = sb("ones_col", [128, 1])
    dst_rows = sb("dst_rows", [ROWS, ROW], INT32)
    dst_next = sb("dst_next", [ROWS, 1], INT32)
    dst_rows_f = sb("dst_rows_f", [ROWS, ROW + 1])
    last_col = sb("last_col", [ROWS, 1])
    unsorted = sb("unsorted", [ROWS, ROW])
    range_node = sb("range_node", [GROUPS, K + 1])
    before = sb("before", [GROUPS, K + 1, ROW])
    row_count = sb("row_count", [GROUPS, K + 1])
    row_index = sb("row_index", [GROUPS, K + 1], INT32)
    row_first = sb("row_first", [GROUPS, K + 1])
    found_row = sb("found_row", [GROUPS, K + 1, ROW])
    before_in_row = sb("before_in_row", [GROUPS, K + 1, ROW])
    in_row = sb("in_row", [GROUPS, K + 1])
    edge_start = sb("edge_start", [GROUPS, K + 1])
    window_start = sb("window_start", [GROUPS, K])
    window_start_i = sb("window_start_i", [GROUPS, K], INT32)
    window = sb("window", [GROUPS, K, EW, 2])
    window_dst = sb("window_dst", [GROUPS, K, EW])
    too_many = sb("too_many", [GROUPS, K])
    violations = sb("violations", [128, 2])
    general_f = sb("general_f", [1, 1])

    dst_loaded = sem("dst_loaded")
    next_loaded = sem("next_loaded")
    weights_loaded = sem("weights_loaded")
    pool_consts = sem("pool_consts")
    ident_ready = sem("ident_ready")
    vec = sem("vec")
    last_col_ready = sem("last_col_ready")
    last_of_rows = sem("last_of_rows")
    eps_ready = sem("eps_ready")
    table_mark = sb("table_mark", [128, 1])
    row_index_ready = sem("row_index_ready")
    row_found = [sem(f"row_found{k}") for k in range(K + 1)]
    starts_ready = sem("starts_ready")
    window_loaded = [sem(f"window_loaded{k}") for k in range(K)]
    window_dst_ready = sem("window_dst_ready")
    window_T_ready = sem("window_T_ready")
    flags_ready = sem("flags_ready")
    flags_summed = sem("flags_summed")
    starts_row_ready = sem("starts_row_ready")

    with nc.Block() as block:
        @block.sync
        def _(sp):
            sp.dma_start(dst_rows[:, :], dst.rearrange("(r e) -> r e", e=ROW)).then_inc(dst_loaded, 16)
            sp.dma_start(dst_next[0:ROWS - 1, :], bass.AP(dst.tensor, ROW, [[ROW, ROWS - 1], [1, 1]]),
                         allow_slow_non_contiguous=True).then_inc(next_loaded, 16)
            sp.dma_start(dst_next[ROWS - 1:ROWS, :], dst[edges - 1:edges].rearrange("(a e) -> a e", a=1)).then_inc(next_loaded, 16)
            sp.dma_start(c["w1_sb"][:, :], w1).then_inc(weights_loaded, 16)
            sp.dma_start(c["w2_sb"][:, :, :], w2.rearrange("(c p) n -> p c n", p=128)).then_inc(weights_loaded, 16)
            for h in range(HC):
                sp.dma_start(c["b1_sb"][:, h:h + 1], b1[h * 128:(h + 1) * 128].rearrange("(p a) -> p a", a=1)).then_inc(weights_loaded, 16)
            sp.dma_start(b2_sb[:, 0, :], b2.rearrange("(a n) -> a n", a=1).to_broadcast([128, b2.shape[0]])).then_inc(weights_loaded, 16)
            sp.wait_ge(weights_loaded, 16 * (3 + HC))
            sp.wait_ge(next_loaded, 32)
            for g in range(X_AHEAD):
                start_x(sp, x, g, g, c)
            sp.wait_ge(starts_row_ready, 1)
            for g in range(EA_FIRST):
                start_edge_attr(sp, edge_attr, window_starts(nc, g, c), g, c)

        @block.gpsimd
        def _(pool):
            for k in range(K + 1):
                nc.gpsimd.iota(range_node[:, k:k + 1], pattern=[[0, 1]], base=0, channel_multiplier=G,
                               allow_small_or_imprecise_dtypes=True).then_inc(pool_consts, 1)
            nc.gpsimd.memset(ident[:, :], 0.0).then_inc(pool_consts, 1)
            pool.wait_ge(pool_consts, K + 2)
            nc.gpsimd.affine_select(out=ident[:, :], in_=ident[:, :], compare_op=ALU.not_equal, fill=1.0,
                                    base=0, pattern=[[-1, 128]], channel_multiplier=1).then_inc(ident_ready, 1)
            nc.gpsimd.iota(node_in_range[:, 0, :].rearrange("p (t q) -> p t q", t=T), pattern=[[1, T], [T, WP]], base=0,
                           channel_multiplier=0, allow_small_or_imprecise_dtypes=True).then_inc(pool_consts, 1)
            pool.wait_ge(row_index_ready, 1)
            for k in range(K + 1):
                nc.gpsimd.indirect_dma_start(
                    out=found_row[:, k, :], out_offset=None, in_=dst.rearrange("(r e) -> r e", e=ROW),
                    in_offset=bass.IndirectOffsetOnAxis(ap=row_index[:, k:k + 1], axis=0)).then_inc(row_found[k], 16)
            pool.wait_ge(starts_ready, 1)
            for k in range(K):
                nc.gpsimd.indirect_dma_start(
                    out=window[:, k, :, :].rearrange("g e a -> g (e a)"), out_offset=None, in_=pairs,
                    in_offset=bass.IndirectOffsetOnAxis(ap=window_start_i[:, k:k + 1], axis=0)).then_inc(window_loaded[k], 16)

        @block.vector
        def _(dve):
            chain = [0]

            def link(ins):
                chain[0] += 1
                ins.then_inc(vec, 1)
                dve.wait_ge(vec, chain[0])

            nc.vector.memset(eps_col[:, :], LN_EPS).then_inc(eps_ready, 1)
            nc.vector.memset(ones_col[:, :], 1.0)
            dve.wait_ge(pool_consts, K + 1)
            for k in range(K + 1):
                last = nc.vector.tensor_scalar(range_node[:, k:k + 1], range_node[:, k:k + 1], float(LAST_BASE), float(T * P0[k]),
                                               ALU.min, ALU.add)
            link(last)
            dve.wait_ge(dst_loaded, 16)
            nc.vector.tensor_copy(last_col[:, :], dst_rows[:, ROW - 1:ROW]).then_inc(last_col_ready, 1)
            dve.wait_ge(last_of_rows, 1)
            for k in range(K + 1):
                last = nc.vector.tensor_scalar(before[:, k, 0:ROWS], prep_ps[0][0:GROUPS, 0:ROWS], range_node[:, k:k + 1], None,
                                               ALU.is_lt, ALU.add, accum_out=row_count[:, k:k + 1])
            link(last)
            nc.vector.tensor_scalar(row_index[:, :], row_count[:, :], float(ROWS - 1), None, ALU.min).then_inc(row_index_ready, 1)
            link(nc.vector.tensor_scalar(row_first[:, :], row_count[:, :], float(ROWS - 1), float(ROW), ALU.min, ALU.mult))
            nc.vector.memset(violations[:, :], 0.0)
            nc.vector.tensor_copy(dst_rows_f[:, 0:ROW], dst_rows[:, :])
            dve.wait_ge(next_loaded, 32)
            link(nc.vector.tensor_copy(dst_rows_f[:, ROW:ROW + 1], dst_next[:, :]))
            link(nc.vector.tensor_tensor(unsorted[:, :], dst_rows_f[:, 0:ROW], dst_rows_f[:, 1:ROW + 1], ALU.is_gt))
            link(nc.vector.reduce_max(violations[0:ROWS, 0:1], unsorted[:, :], AX_X))
            for k in range(K + 1):
                dve.wait_ge(row_found[k], 16)
                last = nc.vector.tensor_scalar(before_in_row[:, k, :], found_row[:, k, :], range_node[:, k:k + 1], None,
                                               ALU.is_lt, ALU.add, accum_out=in_row[:, k:k + 1])
            link(last)
            link(nc.vector.tensor_tensor(edge_start[:, :], row_first[:, :], in_row[:, :], ALU.add))
            nc.vector.tensor_scalar(window_start_i[:, :], edge_start[:, 0:K], float(LAST_WINDOW), None, ALU.min).then_inc(starts_ready, 1)
            link(nc.vector.tensor_scalar(window_start[:, :], edge_start[:, 0:K], float(LAST_WINDOW), None, ALU.min))
            link(nc.vector.tensor_tensor(too_many[:, :], edge_start[:, 1:K + 1], window_start[:, :], ALU.subtract))
            link(nc.vector.tensor_scalar(too_many[:, :], too_many[:, :], float(EW), None, ALU.is_gt))
            nc.vector.reduce_max(violations[0:GROUPS, 1:2], too_many[:, :], AX_X).then_inc(flags_ready, 1)
            dve.wait_ge(flags_summed, 1)
            nc.vector.tensor_copy(c["starts_row"][:, :, 0:K].rearrange("a g k -> a k g"),
                                  prep_ps[1][0:1, 2:2 + K * GROUPS].rearrange("a (k g) -> a k g", k=K)).then_inc(starts_row_ready, 1)
            link(nc.vector.reduce_max(general_f[:, :], prep_ps[1][0:1, 0:2], AX_X))
            nc.vector.tensor_copy(c["general"][:, :], general_f[:, :])
            for k in range(K):
                dve.wait_ge(window_loaded[k], 16)
                nc.vector.tensor_scalar(window_dst[:, k, :], window[:, k, :, 1], range_node[:, k:k + 1], None,
                                        ALU.subtract).then_inc(window_dst_ready, 1)
            for k in range(K):
                dve.wait_ge(window_T_ready, k + 1)
                nc.vector.tensor_copy(c["src_of"][:, :, k], window_ps[k][:, 0, 0:GROUPS])
                nc.vector.tensor_copy(c["dst_of"][:, :, k], window_ps[k][:, 1, 0:GROUPS])

        @block.scalar
        def _(act):
            act.wait_ge(eps_ready, 1)
            nc.scalar.activation(table_mark[:, :], eps_col[:, :], ACT.Sqrt)

        @block.tensor
        def _(pe):
            pe.wait_ge(ident_ready, 1)
            pe.wait_ge(last_col_ready, 1)
            nc.tensor.matmul(prep_ps[0][0:GROUPS, 0:ROWS], last_col[:, :].to_broadcast([ROWS, GROUPS]),
                             ident[0:ROWS, 0:ROWS], start=True, stop=True).then_inc(last_of_rows, 1)
            pe.wait_ge(flags_ready, 1)
            nc.tensor.matmul(prep_ps[1][0:1, 0:2], ones_col[:, :], violations[:, :], start=True, stop=True)
            for k in range(K):
                last = nc.tensor.matmul(prep_ps[1][0:1, 2 + k * GROUPS:2 + (k + 1) * GROUPS], window_start[:, k:k + 1],
                                        ident[0:GROUPS, 0:GROUPS], start=True, stop=True)
            last.then_inc(flags_summed, 1)
            for k in range(K):
                pe.wait_ge(window_dst_ready, k + 1)
                nc.tensor.transpose(window_ps[k][:, 0, 0:GROUPS], window[:, k, :, 0], ident[0:GROUPS, 0:GROUPS])
                nc.tensor.transpose(window_ps[k][:, 1, 0:GROUPS], window_dst[:, k, :], ident[0:GROUPS, 0:GROUPS]).then_inc(window_T_ready, 1)


def main_path(nc, x, edge_attr, out, c, sb, sem):
    D = x.shape[1]
    GROUPS, LAST_BASE, LAST_WINDOW, HC = c["GROUPS"], c["LAST_BASE"], c["LAST_WINDOW"], c["HC"]
    ident, eps_col, b2_sb, node_in_range = c["ident"], c["eps_col"], c["b2_sb"], c["node_in_range"]
    w1_sb, b1_sb, w2_sb = c["w1_sb"], c["b1_sb"], c["w2_sb"]
    starts_row, src_of, dst_of = c["starts_row"], c["src_of"], c["dst_of"]
    hT_ps, h1T_ps, h2_ps = c["hT_ps"], c["h1T_ps"], c["h2_ps"]

    x_sb, pre_msg, x_loaded, ea_loaded = c["x_sb"], c["pre_msg"], c["x_loaded"], c["ea_loaded"]
    LOOPS = (GROUPS - EA_AHEAD) // U

    src_idx = sb("src_idx", [128, U, K], INT32)
    msg_hi = sb("msg_hi", [128, U, K, D], FP32R)
    msg_lo = sb("msg_lo", [128, U, K, D], FP32R)
    sel = sb("sel", [128, U, K, T * WP], FP32R)
    hT = sb("hT", [128, T, 128])
    h1T = sb("h1T", [128, HC, T, 128])
    h2 = sb("h2", [128, 2, T, D])
    z = sb("z", [128, U, T, D])
    y = sb("y", [128, U, T, D])
    stats = sb("stats", [128, U, T, 6])
    mean_var = sb("mean_var", [128, U, T, 2])
    std = sb("std", [128, U, T])
    rstd = sb("rstd", [128, U, T])
    shift = sb("shift", [128, U, T])

    xsrc_added = [sem(f"xsrc_added{u}") for u in range(U)]
    out_stored = [sem(f"out_stored{u}") for u in range(U)]
    idx_copied = sem("idx_copied")
    msg_hi_ready = sem("msg_hi_ready")
    msg_lo_ready = sem("msg_lo_ready")
    sel_ready = sem("sel_ready")
    hT_summed = sem("hT_summed")
    hT_copied = sem("hT_copied")
    h1_summed = sem("h1_summed")
    h1_ready = sem("h1_ready")
    h2_summed = sem("h2_summed")
    h2_ready = sem("h2_ready")
    z_ready = sem("z_ready")
    stats_ready = sem("stats_ready")
    var_ready = sem("var_ready")
    std_ready = sem("std_ready")
    rstd_ready = sem("rstd_ready")
    shift_ready = sem("shift_ready")
    y_ready = sem("y_ready")

    def steps(engine, step):
        for u in range(U):
            step(u, u, 0)
        with engine.Fori(1, LOOPS) as i:
            for u in range(U):
                step(i * U + u, u, i)
        for g in range(LOOPS * U, GROUPS):
            step(g, g % U, g // U)

    def has(g, ahead):
        return not known(g) or 0 <= g + ahead < GROUPS

    def reused(g):
        return not known(g) or g >= U

    with nc.Block() as block:
        @block.sync
        def _(sp):
            def load_x(g, slot):
                if reused(g):
                    sp.wait_ge(z_ready, g - (U - 1))
                start_x(sp, x, g, slot, c)

            def load_ea(g, slot, starts):
                if reused(g):
                    sp.wait_ge(msg_lo_ready, g - (U - 1))
                start_edge_attr(sp, edge_attr, starts, slot, c)

            for g in range(EA_FIRST, EA_AHEAD):
                load_ea(g, g % U, window_starts(nc, g, c))

            def step(g, slot, n):
                starts = window_starts(nc, g + EA_AHEAD, c) if has(g, EA_AHEAD) else None
                if has(g, X_AHEAD):
                    load_x(g + X_AHEAD, (slot + X_AHEAD) % U)
                if has(g, EA_AHEAD):
                    load_ea(g + EA_AHEAD, (slot + EA_AHEAD) % U, starts)
            steps(sp, step)
            for slot in range(U):
                sp.wait_ge(out_stored[slot], 16 * len(range(slot, GROUPS, U)))

        @block.gpsimd
        def _(pool):
            def copy_indices(g, slot):
                nc.gpsimd.tensor_copy(src_idx[:, slot, :], src_of[:, bass.ds(g, 1), :].rearrange("p a k -> p (a k)")).then_inc(idx_copied, 1)

            def gather(g, slot, n):
                pool.wait_ge(idx_copied, g + 1)
                pool.wait_ge(ea_loaded[slot], (n + 1) * (16 * K))
                if has(g, 1):
                    if reused(g + 1):
                        pool.wait_ge(xsrc_added[(slot + 1) % U], (n if slot < U - 1 else n + 1) * (16 * K))
                    copy_indices(g + 1, (slot + 1) % U)
                for k in range(K):
                    nc.gpsimd.indirect_dma_start(
                        out=pre_msg[:, slot, k, :], out_offset=None, in_=x,
                        in_offset=bass.IndirectOffsetOnAxis(ap=src_idx[:, slot, k:k + 1], axis=0),
                        compute_op=ALU.add).then_inc(xsrc_added[slot], 16)
            copy_indices(0, 0)
            steps(pool, gather)

        @block.vector
        def _(dve):
            def select(g, slot):
                if reused(g):
                    dve.wait_ge(hT_summed, g - (U - 1))
                nc.vector.tensor_tensor(sel[:, slot, :, :], node_in_range[:, :, :].to_broadcast([128, K, T * WP]),
                                        dst_of[:, bass.ds(g, 1), :].rearrange("p a k -> p k a").to_broadcast([128, K, T * WP]),
                                        ALU.is_equal).then_inc(sel_ready, 1)

            def low_part(g, slot):
                if reused(g):
                    dve.wait_ge(hT_summed, g - (U - 1))
                dve.wait_ge(msg_hi_ready, g + 1)
                nc.vector.scalar_tensor_tensor(msg_lo[:, slot, :, :], pre_msg[:, slot, :, :], 0.0, msg_hi[:, slot, :, :].bitcast(FP32),
                                               ALU.max, ALU.subtract).then_inc(msg_lo_ready, 1)

            def add_bias(g, slot):
                dve.wait_ge(h2_summed, g + 1)
                nc.vector.tensor_tensor(h2[:, slot % 2, :, :], h2_ps[slot % 2][:, :, :], b2_sb[:, :, :].to_broadcast([128, T, D]),
                                        ALU.add).then_inc(h2_ready, 1)

            def add_x(g, slot):
                if reused(g):
                    dve.wait_ge(y_ready, g - (U - 1))
                dve.wait_ge(h2_ready, g + 1)
                nc.vector.scalar_tensor_tensor(z[:, slot, :, :], h2[:, slot % 2, :, :], 0.0, x_sb[:, slot, :, :],
                                               ALU.max, ALU.add).then_inc(z_ready, 1)

            def statistics(g, slot):
                dve.wait_ge(z_ready, g + 1)
                for t in range(T):
                    last = nc.vector.bn_stats(stats[:, slot, t, :], z[:, slot, t, :])
                last.then_inc(stats_ready, 1)

            def aggregate(g, slot):
                for t in range(T):
                    last = nc.vector.bn_aggr(mean_var[:, slot, t, :], stats[:, slot, t, :])
                last.then_inc(var_ready, 1)

            def reciprocal(g, slot):
                dve.wait_ge(std_ready, g + 1)
                nc.vector.reciprocal(rstd[:, slot, :], std[:, slot, :]).then_inc(rstd_ready, 1)

            def shifts(g, slot):
                dve.wait_ge(rstd_ready, g + 1)
                nc.vector.scalar_tensor_tensor(shift[:, slot, :], mean_var[:, slot, :, 0], -1.0, rstd[:, slot, :],
                                               ALU.mult, ALU.mult).then_inc(shift_ready, 1)

            for g in range(2):
                select(g, g)
            for g in range(2):
                low_part(g, g)
            select(2, 2)

            def step(g, slot, n):
                add_bias(g, slot)
                if has(g, 2):
                    low_part(g + 2, (slot + 2) % U)
                add_x(g, slot)
                if has(g, -1):
                    reciprocal(g - 1, (slot - 1) % U)
                statistics(g, slot)
                dve.wait_ge(stats_ready, g + 1)
                if has(g, 3):
                    select(g + 3, (slot + 3) % U)
                aggregate(g, slot)
                if has(g, -1):
                    shifts(g - 1, (slot - 1) % U)
            steps(dve, step)
            reciprocal(GROUPS - 1, (GROUPS - 1) % U)
            shifts(GROUPS - 1, (GROUPS - 1) % U)

        @block.scalar
        def _(act):
            def high_part(g, slot, n):
                act.wait_ge(xsrc_added[slot], (n + 1) * (16 * K))
                if reused(g):
                    act.wait_ge(hT_summed, g - (U - 1))
                nc.scalar.activation(msg_hi[:, slot, :, :], pre_msg[:, slot, :, :], ACT.Relu).then_inc(msg_hi_ready, 1)

            def copy_hT(g):
                act.wait_ge(hT_summed, g + 1)
                nc.scalar.activation(hT[:, :, :], hT_ps[:, :, :], ACT.Copy).then_inc(hT_copied, 1)

            def hidden(g):
                for h in range(HC):
                    act.wait_ge(h1_summed, g * HC + h + 1)
                    nc.scalar.activation(h1T[:, h, :, :], h1T_ps[h][:, :, :], ACT.Relu, bias=b1_sb[:, h:h + 1]).then_inc(h1_ready, 1)

            def deviation(g, slot):
                act.wait_ge(var_ready, g + 1)
                nc.scalar.activation(std[:, slot, :], mean_var[:, slot, :, 1], ACT.Sqrt, bias=eps_col[:, :]).then_inc(std_ready, 1)

            def normalize(g, slot, n):
                act.wait_ge(shift_ready, g + 1)
                if reused(g):
                    act.wait_ge(out_stored[slot], n * 16)
                for t in range(T):
                    last = nc.scalar.activation(y[:, slot, t, :], z[:, slot, t, :], ACT.Identity,
                                                bias=shift[:, slot, t:t + 1], scale=rstd[:, slot, t:t + 1])
                last.then_inc(y_ready, 1)

            def store(g, slot):
                act.wait_ge(y_ready, g + 1)
                if known(g) and g == GROUPS - 1:
                    act.wait_ge(out_stored[(slot - 1) % U], 16 * ((g - 1) // U + 1))
                act.dma_start(rows(out, g, c), y[:, slot, :, :]).then_inc(out_stored[slot], 16)

            high_part(0, 0, 0)
            copy_hT(0)
            for g in (1, 2):
                high_part(g, g, 0)

            def step(g, slot, n):
                hidden(g)
                if has(g, -3):
                    store(g - 3, (slot - 3) % U)
                if has(g, 1):
                    copy_hT(g + 1)
                if has(g, -1):
                    deviation(g - 1, (slot - 1) % U)
                if has(g, 3):
                    high_part(g + 3, (slot + 3) % U, n if slot < 1 else n + 1)
                if has(g, -2):
                    normalize(g - 2, (slot - 2) % U, n if slot >= 2 else n - 1)
            steps(act, step)
            deviation(GROUPS - 1, (GROUPS - 1) % U)
            store(GROUPS - 3, (GROUPS - 3) % U)
            for g in (GROUPS - 2, GROUPS - 1):
                normalize(g, g % U, g // U)
                store(g, g % U)

        @block.tensor
        def _(pe):
            def sum_hT(g, slot, n):
                pe.wait_ge(x_loaded[slot], (n + 1) * 16)
                for t in range(T):
                    nc.tensor.matmul(hT_ps[:, t, :], x_sb[:, slot, t, :], ident[:, :], is_transpose=True,
                                     start=(t == 0), stop=False, skip_group_check=True)
                pe.wait_ge(sel_ready, g + 1)
                pe.wait_ge(msg_lo_ready, g + 1)
                for k in range(K):
                    p0, p1 = P0[k], P0[k + 1]
                    cols = sel[:, slot, k, :].rearrange("p (t q) -> p t q", t=T)[:, :, 0:p1 - p0]
                    for part in (msg_hi, msg_lo):
                        last = nc.tensor.matmul(hT_ps[:, :, p0:p1], part[:, slot, k, :], cols,
                                                start=False, stop=(k == K - 1), skip_group_check=True)
                last.then_inc(hT_summed, 1)

            sum_hT(0, 0, 0)

            def step(g, slot, n):
                pe.wait_ge(hT_copied, g + 1)
                for h in range(HC):
                    nc.tensor.matmul(h1T_ps[h][:, :, :], w1_sb[:, h * 128:(h + 1) * 128], hT[:, :, :],
                                     start=True, stop=True).then_inc(h1_summed, 1)
                if has(g, 1):
                    sum_hT(g + 1, (slot + 1) % U, n if slot + 1 < U else n + 1)
                if has(g, -2):
                    pe.wait_ge(h2_ready, g - 1)
                for h in range(HC):
                    pe.wait_ge(h1_ready, g * HC + h + 1)
                    for t in range(T):
                        last = nc.tensor.matmul(h2_ps[slot % 2][:, t, :], h1T[:, h, t, :], w2_sb[:, h, :],
                                                start=(h == 0 and t == 0), stop=(h == HC - 1), skip_group_check=True)
                last.then_inc(h2_summed, 1)
            steps(pe, step)


def general_path(nc, x, pairs, edge_attr, out, h_dram, c, sb, sem):
    nodes, D = x.shape
    edges = edge_attr.shape[0]
    HC = c["w2_sb"].shape[1]
    ET = 125
    NT = 125
    EDGE_TILES, NODE_TILES = edges // ET, nodes // NT
    assert EDGE_TILES * ET == edges and NODE_TILES * NT == nodes
    SKIP = float(1 << 20)

    src_dst = sb("g_src_dst", [ET, 2], INT32)
    src_col = src_dst[:, 0:1]
    dst_col = src_dst[:, 1:2]
    dst_col_f = sb("g_dst_col_f", [ET, 1])
    ea = sb("g_ea", [ET, D])
    xsrc = sb("g_xsrc", [ET, D])
    pre_msg = sb("g_pre_msg", [ET, D])
    msg = sb("g_msg", [ET, D])
    pool_mark = sb("g_pool_mark", [1, 2])
    before = sb("g_before", [ET, ET])
    same = sb("g_same", [ET, ET])
    same_before = sb("g_same_before", [ET, ET])
    repeats = sb("g_repeats", [ET, 1])
    target_f = sb("g_target_f", [ET, 1])
    target = sb("g_target", [ET, 1], INT32)
    h_old = sb("g_h_old", [ET, D])
    h_new = sb("g_h_new", [ET, D])
    x_sb = sb("g_x", [NT, D])
    h_sb = sb("g_h", [NT, D])
    hT = sb("g_hT", [D, NT])
    h1T = sb("g_h1T", [128, HC, NT])
    h2 = sb("g_h2", [NT, D])
    z = sb("g_z", [NT, D])
    stats = sb("g_stats", [NT, 6])
    mean_var = sb("g_mean_var", [NT, 2])
    std = sb("g_std", [NT, 1])
    rstd = sb("g_rstd", [NT, 1])
    y = sb("g_y", [NT, D])

    copied = sem("g_copied")
    marks = sem("g_marks")
    before_ready = sem("g_before_ready")
    edges_loaded = sem("g_edges_loaded")
    xsrc_loaded = sem("g_xsrc_loaded")
    h_old_loaded = sem("g_h_old_loaded")
    dst_f_ready = sem("g_dst_f_ready")
    dst_row_ready = sem("g_dst_row_ready")
    same_ready = sem("g_same_ready")
    repeats_ready = sem("g_repeats_ready")
    masked = sem("g_masked")
    masked_target = sem("g_masked_target")
    target_ready = sem("g_target_ready")
    summed = sem("g_summed")
    msg_ready = sem("g_msg_ready")
    msg_summed = sem("g_msg_summed")
    h_new_ready = sem("g_h_new_ready")
    scattered = sem("g_scattered")
    tile_loaded = sem("g_tile_loaded")
    hT_ready = sem("g_hT_ready")
    hT_copied = sem("g_hT_copied")
    h1_summed = sem("g_h1_summed")
    h1_ready = sem("g_h1_ready")
    h2_summed = sem("g_h2_summed")
    h2_ready = sem("g_h2_ready")
    z_ready = sem("g_z_ready")
    stats_ready = sem("g_stats_ready")
    var_ready = sem("g_var_ready")
    std_ready = sem("g_std_ready")
    rstd_ready = sem("g_rstd_ready")
    y_ready = sem("g_y_ready")
    stored = sem("g_stored")

    dst_row_ps, msg_ps = c["prep_ps"]
    hT_ps, (h1_ps, h2_ps) = c["hT_ps"], c["h1T_ps"]

    with nc.Block() as block:
        @block.sync
        def _(sp):
            sp.dma_start(h_dram.rearrange("(a b) d -> a (b d)", b=NT), x.rearrange("(a b) d -> a (b d)", b=NT)).then_inc(copied, 16)

            def load_edges(first):
                sp.dma_start(src_dst[:, :], pairs[bass.ds(first, ET), :]).then_inc(edges_loaded, 16)
                sp.dma_start(ea[:, :], edge_attr[bass.ds(first, ET), :]).then_inc(edges_loaded, 16)

            load_edges(0)
            with sp.Fori(1, EDGE_TILES) as i:
                sp.wait_ge(scattered, i * 16)
                load_edges(i * ET)
            sp.wait_ge(scattered, EDGE_TILES * 16)

            def load_nodes(first):
                sp.dma_start(x_sb[:, :], x[bass.ds(first, NT), :]).then_inc(tile_loaded, 16)
                sp.dma_start(h_sb[:, :], h_dram[bass.ds(first, NT), :]).then_inc(tile_loaded, 16)

            load_nodes(0)
            with sp.Fori(1, NODE_TILES) as i:
                sp.wait_ge(y_ready, i)
                sp.dma_start(out[bass.ds((i - 1) * NT, NT), :], y[:, :]).then_inc(stored, 16)
                sp.wait_ge(stored, i * 16)
                load_nodes(i * NT)
            sp.wait_ge(y_ready, NODE_TILES)
            sp.dma_start(out[(NODE_TILES - 1) * NT:NODE_TILES * NT, :], y[:, :]).then_inc(stored, 16)
            sp.wait_ge(stored, NODE_TILES * 16)

        @block.gpsimd
        def _(pool):
            nc.gpsimd.memset(before[:, :], 0.0).then_inc(before_ready, 1)
            nc.gpsimd.memset(pool_mark[:, :], 0.0).then_inc(marks, 1)
            pool.wait_ge(marks, 1)
            pool.wait_ge(before_ready, 1)
            nc.gpsimd.affine_select(out=before[:, :], in_=before[:, :], compare_op=ALU.is_ge, fill=1.0,
                                    base=0, pattern=[[1, ET]], channel_multiplier=-1).then_inc(before_ready, 1)
            pool.wait_ge(copied, 16)

            def mark(done):
                pool.wait_ge(marks, done)
                nc.gpsimd.tensor_tensor(pool_mark[:, 1:2], pool_mark[:, 0:1], pool_mark[:, 0:1], ALU.add).then_inc(marks, 1)

            with pool.Fori(0, EDGE_TILES) as i:
                pool.wait_ge(edges_loaded, (i + 1) * 32)
                mark(2 * i + 1)
                nc.gpsimd.indirect_dma_start(out=xsrc[:, :], out_offset=None, in_=x,
                                             in_offset=bass.IndirectOffsetOnAxis(ap=src_col, axis=0)).then_inc(xsrc_loaded, 16)
                nc.gpsimd.indirect_dma_start(out=h_old[:, :], out_offset=None, in_=h_dram,
                                             in_offset=bass.IndirectOffsetOnAxis(ap=dst_col, axis=0)).then_inc(h_old_loaded, 16)
                pool.wait_ge(target_ready, i + 1)
                pool.wait_ge(h_new_ready, i + 1)
                mark(2 * i + 2)
                nc.gpsimd.indirect_dma_start(out=h_dram, out_offset=bass.IndirectOffsetOnAxis(ap=target[:, 0:1], axis=0),
                                             in_=h_new[:, :], in_offset=None,
                                             bounds_check=nodes - 1, oob_is_err=False).then_inc(scattered, 16)

        @block.vector
        def _(dve):
            dve.wait_ge(before_ready, 2)
            with dve.Fori(0, EDGE_TILES) as i:
                n = i + 1
                dve.wait_ge(edges_loaded, n * 32)
                nc.vector.tensor_copy(dst_col_f[:, :], dst_col).then_inc(dst_f_ready, 1)
                dve.wait_ge(dst_f_ready, n)
                dve.wait_ge(dst_row_ready, n)
                nc.vector.tensor_scalar(same[:, :], dst_row_ps[0:ET, 0:ET], dst_col_f[:, 0:1], None, ALU.is_equal).then_inc(same_ready, 1)
                dve.wait_ge(same_ready, n)
                nc.vector.tensor_tensor(same_before[:, :], same[:, :], before[:, :], ALU.mult).then_inc(masked, 1)
                dve.wait_ge(masked, n)
                nc.vector.reduce_max(repeats[:, :], same_before[:, :], AX_X).then_inc(repeats_ready, 1)
                dve.wait_ge(repeats_ready, n)
                nc.vector.scalar_tensor_tensor(target_f[:, :], repeats[:, :], SKIP, dst_col_f[:, :], ALU.mult, ALU.add).then_inc(masked_target, 1)
                dve.wait_ge(masked_target, n)
                nc.vector.tensor_copy(target[:, :], target_f[:, :]).then_inc(target_ready, 1)
                dve.wait_ge(xsrc_loaded, n * 16)
                nc.vector.tensor_tensor(pre_msg[:, :], ea[:, :], xsrc[:, :], ALU.add).then_inc(summed, 1)
                dve.wait_ge(summed, n)
                nc.vector.tensor_scalar(msg[:, :], pre_msg[:, :], 0.0, None, ALU.max).then_inc(msg_ready, 1)
                dve.wait_ge(h_old_loaded, n * 16)
                dve.wait_ge(msg_summed, n)
                nc.vector.tensor_tensor(h_new[:, :], msg_ps[0:ET, 0:D], h_old[:, :], ALU.add).then_inc(h_new_ready, 1)
            with dve.Fori(0, NODE_TILES) as i:
                n = i + 1
                dve.wait_ge(tile_loaded, n * 32)
                dve.wait_ge(h2_summed, n)
                nc.vector.tensor_tensor(h2[:, :], h2_ps[0:NT, 0, :], c["b2_sb"][0:NT, 0, :], ALU.add).then_inc(h2_ready, 1)
                dve.wait_ge(h2_ready, n)
                nc.vector.scalar_tensor_tensor(z[:, :], h2[:, :], 0.0, x_sb[:, :], ALU.max, ALU.add).then_inc(z_ready, 1)
                dve.wait_ge(z_ready, n)
                nc.vector.bn_stats(stats[:, :], z[:, :]).then_inc(stats_ready, 1)
                dve.wait_ge(stats_ready, n)
                nc.vector.memset(rstd[:, :], 0.0)
                nc.vector.bn_aggr(mean_var[:, :], stats[:, :]).then_inc(var_ready, 1)
                dve.wait_ge(std_ready, n)
                nc.vector.reciprocal(rstd[:, :], std[:, :]).then_inc(rstd_ready, 1)
                dve.wait_ge(rstd_ready, n)
                nc.vector.tensor_scalar(y[:, :], z[:, :], mean_var[:, 0:1], rstd[:, 0:1], ALU.subtract, ALU.mult).then_inc(y_ready, 1)

        @block.scalar
        def _(act):
            with act.Fori(0, NODE_TILES) as i:
                n = i + 1
                act.wait_ge(hT_ready, n)
                nc.scalar.activation(hT[:, :], hT_ps[:, 0, 0:NT], ACT.Copy).then_inc(hT_copied, 1)
                act.wait_ge(h1_summed, n)
                for k in range(HC):
                    last = nc.scalar.activation(h1T[:, k, :], h1_ps[:, k, 0:NT], ACT.Relu, bias=c["b1_sb"][:, k:k + 1])
                last.then_inc(h1_ready, 1)
                act.wait_ge(var_ready, n)
                nc.scalar.activation(std[:, :], mean_var[:, 1:2], ACT.Sqrt, bias=c["eps_col"][0:NT, :]).then_inc(std_ready, 1)

        @block.tensor
        def _(pe):
            with pe.Fori(0, EDGE_TILES) as i:
                n = i + 1
                pe.wait_ge(dst_f_ready, n)
                nc.tensor.matmul(dst_row_ps[0:ET, 0:ET], dst_col_f[:, 0:1].to_broadcast([ET, ET]), c["ident"][0:ET, 0:ET],
                                 start=True, stop=True).then_inc(dst_row_ready, 1)
                pe.wait_ge(same_ready, n)
                pe.wait_ge(msg_ready, n)
                nc.tensor.matmul(msg_ps[0:ET, 0:D], same[:, :], msg[:, :], start=True, stop=True).then_inc(msg_summed, 1)
            with pe.Fori(0, NODE_TILES) as i:
                n = i + 1
                pe.wait_ge(tile_loaded, n * 32)
                nc.tensor.transpose(hT_ps[:, 0, 0:NT], h_sb[:, :], c["ident"][0:NT, 0:NT]).then_inc(hT_ready, 1)
                pe.wait_ge(hT_copied, n)
                for k in range(HC):
                    last = nc.tensor.matmul(h1_ps[:, k, 0:NT], c["w1_sb"][:, k * 128:(k + 1) * 128], hT[:, :], start=True, stop=True)
                last.then_inc(h1_summed, 1)
                pe.wait_ge(h1_ready, n)
                for k in range(HC):
                    last = nc.tensor.matmul(h2_ps[0:NT, 0, :], h1T[:, k, :], c["w2_sb"][:, k, :], start=(k == 0), stop=(k == HC - 1))
                last.then_inc(h2_summed, 1)


def gnn_resnorm_kernel(nc, x, dst, pairs, edge_attr, w1, b1, w2, b2, out, h_dram):
    nodes, D = x.shape
    edges = edge_attr.shape[0]
    hidden = w1.shape[1]
    HC = hidden // 128
    GROUPS = -(-nodes // G)
    assert D == 128 and HC * 128 == hidden

    ctx = ExitStack()
    with ctx:
        def sb(name, shape, dt=FP32):
            return ctx.enter_context(nc.sbuf_tensor(name, shape, dt))

        def pb(name, shape, dt=FP32):
            return ctx.enter_context(nc.psum_tensor(name, shape, dt))

        def sem(name):
            return ctx.enter_context(nc.semaphore(name))

        c = dict(
            GROUPS=GROUPS, LAST_BASE=nodes - G, LAST_WINDOW=edges - EW, HC=HC,
            ident=sb("ident", [128, 128]),
            eps_col=sb("eps_col", [128, 1]),
            w1_sb=sb("w1_sb", [128, hidden]),
            b1_sb=sb("b1_sb", [128, HC]),
            w2_sb=sb("w2_sb", [128, HC, D]),
            b2_sb=sb("b2_sb", [128, 1, D]),
            node_in_range=sb("node_in_range", [128, 1, T * WP]),
            src_of=sb("src_of", [128, GROUPS, K], INT32),
            dst_of=sb("dst_of", [128, GROUPS, K]),
            starts_row=sb("starts_row", [1, GROUPS, 4], INT32),
            general=sb("general", [1, 1], INT32),
            pre_msg=sb("pre_msg", [128, U, K, D]),
            x_sb=sb("x_sb", [128, U, T, D]),
            ea_loaded=[sem(f"ea_loaded{u}") for u in range(U)],
            x_loaded=[sem(f"x_loaded{u}") for u in range(U)],
            hT_ps=pb("hT_ps", [128, T, 128]),
            h1T_ps=[pb(f"h1T_ps{h}", [128, T, 128]) for h in range(HC)],
            h2_ps=[pb(f"h2_ps{i}", [128, T, D]) for i in range(2)],
            prep_ps=[pb(f"prep_ps{i}", [128, 512]) for i in range(2)],
        )
        prepare(nc, x, edge_attr, dst, pairs, w1, b1, w2, b2, c, sb, sem)

        windows_fail = nc.values_load(c["general"][0:1, 0:1], min_val=0, max_val=128)
        with nc.If(windows_fail == 0):
            main_path(nc, x, edge_attr, out, c, sb, sem)
        with nc.Else():
            general_path(nc, x, pairs, edge_attr, out, h_dram, c, sb, sem)


def kernel(**inputs):
    import numpy as _np
    import concourse.bacc as _bacc
    from concourse import mybir as _mybir
    from concourse.bass_utils import run_bass_kernel_spmd as _run

    nc = _bacc.Bacc("TRN2", target_bir_lowering=False, num_devices=1)
    laid = {
        "x": inputs["x"],
        "dst": inputs["dst"],
        "pairs": _np.stack([inputs["src"], inputs["dst"]], axis=1),
        "edge_attr": inputs["edge_attr_128"],
        "w1": inputs["L0_gnn_W1"],
        "b1": inputs["L0_gnn_b1"],
        "w2": inputs["L0_gnn_W2"],
        "b2": inputs["L0_gnn_b2"],
    }
    arrays, args = {}, []
    for name, a in laid.items():
        a = _np.ascontiguousarray(a)
        arrays[f"in_{name}_dram"] = a
        args.append(nc.dram_tensor(f"in_{name}_dram", a.shape, _mybir.dt.from_np(a.dtype), kind="ExternalInput").ap())
    shape = inputs["x"].shape
    out = nc.dram_tensor("out_dram", shape, _mybir.dt.float32, kind="ExternalOutput").ap()
    h_dram = nc.dram_tensor("h_dram", shape, _mybir.dt.float32, kind="Internal").ap()
    gnn_resnorm_kernel(nc, *args, out, h_dram)
    r = _run(nc, [arrays], core_ids=[0])
    return r.results[0]["out_dram"]
```
